# Optimizing a Trainium2 kernel written in Bass

```python
import numpy as np
import jax
import jax.numpy as jnp

def _softmax(x, axis=-1):
    return jax.nn.softmax(x, axis=axis)

def _gelu(x):
    return jax.nn.gelu(x, approximate=True)

def _silu(x):
    return jax.nn.silu(x)

def _sigmoid(x):
    return jax.nn.sigmoid(x)

def _layernorm(x, axis=-1, eps=1e-05):
    m = jnp.mean(x, axis=axis, keepdims=True)
    v = jnp.var(x, axis=axis, keepdims=True)
    return (x - m) / jnp.sqrt(v + eps)

def _scatter_add(tgt, idx, src, axis=0):
    return tgt.at[idx].add(src)

def _segment_sum(src, seg, n):
    return jax.ops.segment_sum(src, seg, n)
kernel_name = 'mk_macaron_d2_jaxref_r8_f7df9a'

def setup_inputs(seed: int=0):
    np.random.seed(seed)
    _w = jnp.asarray

    def _L0_attn_setup():
        import jax, jax.numpy as jnp
        import numpy as np
        import math
        H = 256
        B = 4
        T = 256
        LAYERS = 24
        INDEX = 3
        EPS = 1e-05

        def _layer_norm(x, g, b):
            m = jnp.mean(x, axis=-1, keepdims=True)
            v = jnp.mean((x - m) ** 2, axis=-1, keepdims=True)
            return (x - m) * jax.lax.rsqrt(v + EPS) * g + b

        def _time_shift(x):
            return jnp.pad(x, ((0, 0), (1, 0), (0, 0)))[:, :-1, :]

        def _wkv_run(k, v, tm_first, tm_decay):
            C = k.shape[-1]
            aa = jnp.zeros((C,), k.dtype)
            bb = jnp.zeros((C,), k.dtype)
            pp = jnp.full((C,), -1e+38, k.dtype)
            ww = tm_first + k
            p = jnp.maximum(pp, ww)
            e1 = jnp.exp(pp - p)
            e2 = jnp.exp(ww - p)
            a = e1 * aa + e2 * v
            b = e1 * bb + e2
            return a / b
        key = jax.random.key(seed)
        ks = jax.random.split(key, 9)
        i = jnp.arange(H, dtype=jnp.float32)
        r01 = INDEX / (LAYERS - 1)
        r1pz = 1.0 - INDEX / LAYERS
        tm_decay = -5.0 + 8.0 * (i / (H - 1)) ** (0.7 + 1.3 * r01)
        zigzag = ((jnp.arange(H) + 1) % 3 - 1).astype(jnp.float32) * 0.5
        tm_first = jnp.float32(math.log(0.3)) + zigzag
        xr = i / H
        tm_mk = (xr ** r1pz)[None, None, :]
        tm_mv = tm_mk + 0.3 * r01
        tm_mr = (xr ** (0.5 * r1pz))[None, None, :]
        cm_mk = (xr ** r1pz)[None, None, :]
        cm_mr = (xr ** r1pz)[None, None, :]
        s = 1.0 / math.sqrt(H)
        s4 = 1.0 / math.sqrt(4 * H)
        Wk = jax.random.normal(ks[0], (H, H), jnp.float32) * s
        Wv = jax.random.normal(ks[1], (H, H), jnp.float32) * s
        Wr = jax.random.normal(ks[2], (H, H), jnp.float32) * s
        Wo = jax.random.normal(ks[3], (H, H), jnp.float32) * s
        Wkey = jax.random.normal(ks[4], (4 * H, H), jnp.float32) * s
        Wval = jax.random.normal(ks[5], (H, 4 * H), jnp.float32) * s4
        Wcr = jax.random.normal(ks[6], (H, H), jnp.float32) * s
        x = jax.random.normal(ks[7], (B, T, H), jnp.float32)
        return {'x': x, 'ln1_g': jnp.ones((H,), jnp.float32), 'ln1_b': jnp.zeros((H,), jnp.float32), 'ln2_g': jnp.ones((H,), jnp.float32), 'ln2_b': jnp.zeros((H,), jnp.float32), 'tm_decay': tm_decay, 'tm_first': tm_first, 'tm_mk': tm_mk, 'tm_mv': tm_mv, 'tm_mr': tm_mr, 'Wk': Wk, 'Wv': Wv, 'Wr': Wr, 'Wo': Wo, 'cm_mk': cm_mk, 'cm_mr': cm_mr, 'Wkey': Wkey, 'Wval': Wval, 'Wcr': Wcr}
    _L0_attn_in = _L0_attn_setup()

    def _L0_ffn_setup():
        import jax, jax.numpy as jnp
        import numpy as np
        B, S, D = (4, 64, 256)
        E, K, H = (8, 2, 176)
        HS = 2 * 176
        ALPHA = 0.001
        W_SCALE = 0.02

        def _moe_forward(hidden_states, gate_w, w_gate, w_up, w_down, sw_gate, sw_up, sw_down):
            b, s, d = hidden_states.shape
            x = hidden_states.reshape(-1, d)
            T = x.shape[0]
            logits = x @ gate_w
            scores = jax.nn.softmax(logits, axis=-1)
            topk_w, topk_idx = jax.lax.top_k(scores, K)
            mask = jax.nn.one_hot(topk_idx, E, dtype=scores.dtype).sum(axis=1)
            ce = mask.mean(axis=0)
            Pi = scores.mean(axis=0)
            aux_loss = (Pi * ce * E).sum() * ALPHA
            comb = jnp.zeros((T, E), dtype=x.dtype)
            comb = comb.at[jnp.arange(T)[:, None], topk_idx].add(topk_w)
            g = jax.nn.silu(jnp.einsum('td,edh->teh', x, w_gate)) * jnp.einsum('td,edh->teh', x, w_up)
            routed = jnp.einsum('teh,ehd,te->td', g, w_down, comb)
            shared = jax.nn.silu(x @ sw_gate) * (x @ sw_up) @ sw_down
            out = (routed + shared).reshape(b, s, d)
            return (out, aux_loss)
        key = jax.random.key(seed)
        ks = jax.random.split(key, 8)
        rn = lambda k, sh: jax.random.normal(k, sh, dtype=jnp.float32)
        return {'hidden_states': rn(ks[0], (B, S, D)), 'gate_w': rn(ks[1], (D, E)) * W_SCALE, 'w_gate': rn(ks[2], (E, D, H)) * W_SCALE, 'w_up': rn(ks[3], (E, D, H)) * W_SCALE, 'w_down': rn(ks[4], (E, H, D)) * W_SCALE, 'sw_gate': rn(ks[5], (D, HS)) * W_SCALE, 'sw_up': rn(ks[6], (D, HS)) * W_SCALE, 'sw_down': rn(ks[7], (HS, D)) * W_SCALE}
    _L0_ffn_in = _L0_ffn_setup()

    def _L1_attn_setup():
        import jax, jax.numpy as jnp
        import numpy as np
        ROPE_THETA = 10000.0

        def rope(t, rot_dim):
            S = t.shape[-2]
            half = rot_dim // 2
            inv_freq = 1.0 / ROPE_THETA ** (jnp.arange(0, rot_dim, 2, dtype=jnp.float32) / rot_dim)
            freqs = jnp.arange(S, dtype=jnp.float32)[:, None] * inv_freq[None, :]
            freqs = jnp.repeat(freqs, 2, axis=-1)
            cos, sin = (jnp.cos(freqs), jnp.sin(freqs))
            t_rot, t_pass = (t[..., :rot_dim], t[..., rot_dim:])
            x = t_rot.reshape(*t_rot.shape[:-1], half, 2)
            rh = jnp.stack([-x[..., 1], x[..., 0]], axis=-1).reshape(t_rot.shape)
            t_rot = t_rot * cos + rh * sin
            return jnp.concatenate([t_rot, t_pass], axis=-1)

        def feature_map(x):
            norm = jnp.sqrt(jnp.sum(x * x, axis=-1, keepdims=True))
            return x / jnp.maximum(norm, 1e-12)
        key = jax.random.key(seed)
        kx, kwi, kwo = jax.random.split(key, 3)
        B, S, D = (8, 512, 256)
        scale = 0.02
        return {'X': jax.random.normal(kx, (B, S, D), dtype=jnp.float32), 'W_in': jax.random.normal(kwi, (3 * D, D), dtype=jnp.float32) * scale, 'b_in': jnp.zeros((3 * D,), dtype=jnp.float32), 'W_out': jax.random.normal(kwo, (D, D), dtype=jnp.float32) * scale, 'b_out': jnp.zeros((D,), dtype=jnp.float32)}
    _L1_attn_in = _L1_attn_setup()

    def _L1_ffn_setup():
        import jax, jax.numpy as jnp
        import numpy as np
        HID = 256
        N_EXP = 32
        F_EXP = 96
        TOP_K = 6
        F_SH = 192
        B, S = (1, 128)
        key = jax.random.key(seed)
        ks = jax.random.split(key, 8)
        s = 0.02
        return {'hidden_states': jax.random.normal(ks[0], (B, S, HID), dtype=jnp.float32), 'gate_w': jax.random.normal(ks[1], (HID, N_EXP), dtype=jnp.float32) * s, 'wg': jax.random.normal(ks[2], (N_EXP, HID, F_EXP), dtype=jnp.float32) * s, 'wu': jax.random.normal(ks[3], (N_EXP, HID, F_EXP), dtype=jnp.float32) * s, 'wd': jax.random.normal(ks[4], (N_EXP, F_EXP, HID), dtype=jnp.float32) * s, 'sg': jax.random.normal(ks[5], (HID, F_SH), dtype=jnp.float32) * s, 'su': jax.random.normal(ks[6], (HID, F_SH), dtype=jnp.float32) * s, 'sd': jax.random.normal(ks[7], (F_SH, HID), dtype=jnp.float32) * s}
    _L1_ffn_in = _L1_ffn_setup()
    _d = {'L0_attn_x': _L0_attn_in['x'], 'L0_attn_ln1_g': _L0_attn_in['ln1_g'], 'L0_attn_ln1_b': _L0_attn_in['ln1_b'], 'L0_attn_ln2_g': _L0_attn_in['ln2_g'], 'L0_attn_ln2_b': _L0_attn_in['ln2_b'], 'L0_attn_tm_decay': _L0_attn_in['tm_decay'], 'L0_attn_tm_first': _L0_attn_in['tm_first'], 'L0_attn_tm_mk': _L0_attn_in['tm_mk'], 'L0_attn_tm_mv': _L0_attn_in['tm_mv'], 'L0_attn_tm_mr': _L0_attn_in['tm_mr'], 'L0_attn_Wk': _L0_attn_in['Wk'], 'L0_attn_Wv': _L0_attn_in['Wv'], 'L0_attn_Wr': _L0_attn_in['Wr'], 'L0_attn_Wo': _L0_attn_in['Wo'], 'L0_attn_cm_mk': _L0_attn_in['cm_mk'], 'L0_attn_cm_mr': _L0_attn_in['cm_mr'], 'L0_attn_Wkey': _L0_attn_in['Wkey'], 'L0_attn_Wval': _L0_attn_in['Wval'], 'L0_attn_Wcr': _L0_attn_in['Wcr'], 'L0_ffn_gate_w': _L0_ffn_in['gate_w'], 'L0_ffn_w_gate': _L0_ffn_in['w_gate'], 'L0_ffn_w_up': _L0_ffn_in['w_up'], 'L0_ffn_w_down': _L0_ffn_in['w_down'], 'L0_ffn_sw_gate': _L0_ffn_in['sw_gate'], 'L0_ffn_sw_up': _L0_ffn_in['sw_up'], 'L0_ffn_sw_down': _L0_ffn_in['sw_down'], 'L1_attn_W_in': _L1_attn_in['W_in'], 'L1_attn_b_in': _L1_attn_in['b_in'], 'L1_attn_W_out': _L1_attn_in['W_out'], 'L1_attn_b_out': _L1_attn_in['b_out'], 'L1_ffn_gate_w': _L1_ffn_in['gate_w'], 'L1_ffn_wg': _L1_ffn_in['wg'], 'L1_ffn_wu': _L1_ffn_in['wu'], 'L1_ffn_wd': _L1_ffn_in['wd'], 'L1_ffn_sg': _L1_ffn_in['sg'], 'L1_ffn_su': _L1_ffn_in['su'], 'L1_ffn_sd': _L1_ffn_in['sd']}
    _x0 = _d['L0_attn_x']
    _d['L0_attn_x'] = jax.random.normal(jax.random.fold_in(jax.random.key(seed), 1), (2, 1024, 256), dtype=_x0.dtype)
    del _x0
    return _d

def reference(L0_attn_x, L0_attn_ln1_g, L0_attn_ln1_b, L0_attn_ln2_g, L0_attn_ln2_b, L0_attn_tm_decay, L0_attn_tm_first, L0_attn_tm_mk, L0_attn_tm_mv, L0_attn_tm_mr, L0_attn_Wk, L0_attn_Wv, L0_attn_Wr, L0_attn_Wo, L0_attn_cm_mk, L0_attn_cm_mr, L0_attn_Wkey, L0_attn_Wval, L0_attn_Wcr, L0_ffn_gate_w, L0_ffn_w_gate, L0_ffn_w_up, L0_ffn_w_down, L0_ffn_sw_gate, L0_ffn_sw_up, L0_ffn_sw_down, L1_attn_W_in, L1_attn_b_in, L1_attn_W_out, L1_attn_b_out, L1_ffn_gate_w, L1_ffn_wg, L1_ffn_wu, L1_ffn_wd, L1_ffn_sg, L1_ffn_su, L1_ffn_sd):

    def _L0_attn_ref(x, ln1_g, ln1_b, ln2_g, ln2_b, tm_decay, tm_first, tm_mk, tm_mv, tm_mr, Wk, Wv, Wr, Wo, cm_mk, cm_mr, Wkey, Wval, Wcr):
        import jax, jax.numpy as jnp
        import numpy as np
        import math
        H = 256
        B = 4
        T = 256
        LAYERS = 24
        INDEX = 3
        EPS = 1e-05

        def _layer_norm(x, g, b):
            m = jnp.mean(x, axis=-1, keepdims=True)
            v = jnp.mean((x - m) ** 2, axis=-1, keepdims=True)
            return (x - m) * jax.lax.rsqrt(v + EPS) * g + b

        def _time_shift(x):
            return jnp.pad(x, ((0, 0), (1, 0), (0, 0)))[:, :-1, :]

        def _wkv_run(k, v, tm_first, tm_decay):
            C = k.shape[-1]
            aa = jnp.zeros((C,), k.dtype)
            bb = jnp.zeros((C,), k.dtype)
            pp = jnp.full((C,), -1e+38, k.dtype)
            ww = tm_first + k
            p = jnp.maximum(pp, ww)
            e1 = jnp.exp(pp - p)
            e2 = jnp.exp(ww - p)
            a = e1 * aa + e2 * v
            b = e1 * bb + e2
            return a / b
        h = _layer_norm(x, ln1_g, ln1_b)
        hh = _time_shift(h)
        k = (h * tm_mk + hh * (1 - tm_mk)) @ Wk.T
        v = (h * tm_mv + hh * (1 - tm_mv)) @ Wv.T
        r = (h * tm_mr + hh * (1 - tm_mr)) @ Wr.T
        wkv = _wkv_run(k, v, tm_first, tm_decay)
        x = x + jax.nn.sigmoid(r) * wkv @ Wo.T
        h = _layer_norm(x, ln2_g, ln2_b)
        hh = _time_shift(h)
        kk = (h * cm_mk + hh * (1 - cm_mk)) @ Wkey.T
        kv = jax.nn.silu(kk) @ Wval.T
        sr = jax.nn.sigmoid((h * cm_mr + hh * (1 - cm_mr)) @ Wcr.T)
        x = x + sr * kv
        return x

    def _L0_ffn_ref(hidden_states, gate_w, w_gate, w_up, w_down, sw_gate, sw_up, sw_down):
        import jax, jax.numpy as jnp
        import numpy as np
        B, S, D = (4, 64, 256)
        E, K, H = (8, 2, 176)
        HS = 2 * 176
        ALPHA = 0.001
        W_SCALE = 0.02

        def _moe_forward(hidden_states, gate_w, w_gate, w_up, w_down, sw_gate, sw_up, sw_down):
            b, s, d = hidden_states.shape
            x = hidden_states.reshape(-1, d)
            T = x.shape[0]
            logits = x @ gate_w
            scores = jax.nn.softmax(logits, axis=-1)
            topk_w, topk_idx = jax.lax.top_k(scores, K)
            mask = jax.nn.one_hot(topk_idx, E, dtype=scores.dtype).sum(axis=1)
            ce = mask.mean(axis=0)
            Pi = scores.mean(axis=0)
            aux_loss = (Pi * ce * E).sum() * ALPHA
            comb = jnp.zeros((T, E), dtype=x.dtype)
            comb = comb.at[jnp.arange(T)[:, None], topk_idx].add(topk_w)
            g = jax.nn.silu(jnp.einsum('td,edh->teh', x, w_gate)) * jnp.einsum('td,edh->teh', x, w_up)
            routed = jnp.einsum('teh,ehd,te->td', g, w_down, comb)
            shared = jax.nn.silu(x @ sw_gate) * (x @ sw_up) @ sw_down
            out = (routed + shared).reshape(b, s, d)
            return (out, aux_loss)
        out, _aux = _moe_forward(hidden_states, gate_w, w_gate, w_up, w_down, sw_gate, sw_up, sw_down)
        return out

    def _L1_attn_ref(X, W_in, b_in, W_out, b_out):
        import jax, jax.numpy as jnp
        import numpy as np
        ROPE_THETA = 10000.0

        def rope(t, rot_dim):
            S = t.shape[-2]
            half = rot_dim // 2
            inv_freq = 1.0 / ROPE_THETA ** (jnp.arange(0, rot_dim, 2, dtype=jnp.float32) / rot_dim)
            freqs = jnp.arange(S, dtype=jnp.float32)[:, None] * inv_freq[None, :]
            freqs = jnp.repeat(freqs, 2, axis=-1)
            cos, sin = (jnp.cos(freqs), jnp.sin(freqs))
            t_rot, t_pass = (t[..., :rot_dim], t[..., rot_dim:])
            x = t_rot.reshape(*t_rot.shape[:-1], half, 2)
            rh = jnp.stack([-x[..., 1], x[..., 0]], axis=-1).reshape(t_rot.shape)
            t_rot = t_rot * cos + rh * sin
            return jnp.concatenate([t_rot, t_pass], axis=-1)

        def feature_map(x):
            norm = jnp.sqrt(jnp.sum(x * x, axis=-1, keepdims=True))
            return x / jnp.maximum(norm, 1e-12)
        D = X.shape[-1]
        QKV = jnp.einsum('bsd,ed->bse', X, W_in) + b_in
        Q, K, V = jnp.split(QKV, 3, axis=-1)
        rot_dim = D // 2
        Q = rope(Q, rot_dim)
        K = rope(K, rot_dim)
        A = jnp.sum(feature_map(K) * V, axis=-2)
        Y = A[:, None, :] * Q
        Y = jnp.einsum('bsd,ed->bse', Y, W_out) + b_out
        return Y + X

    def _L1_ffn_ref(hidden_states, gate_w, wg, wu, wd, sg, su, sd):
        import jax, jax.numpy as jnp
        import numpy as np
        HID = 256
        N_EXP = 32
        F_EXP = 96
        TOP_K = 6
        F_SH = 192
        B, S = (1, 128)
        orig_shape = hidden_states.shape
        x = hidden_states.reshape(-1, HID)
        scores = jax.nn.sigmoid(x @ gate_w)
        topk_w, topk_i = jax.lax.top_k(scores, TOP_K)
        topk_w = topk_w / (jnp.sum(topk_w, axis=-1, keepdims=True) + 1e-20)
        combine = jnp.sum(jax.nn.one_hot(topk_i, N_EXP, dtype=topk_w.dtype) * topk_w[..., None], axis=1)
        g = jnp.einsum('td,edf->tef', x, wg)
        u = jnp.einsum('td,edf->tef', x, wu)
        act = jax.nn.silu(g) * u
        routed = jnp.einsum('tef,efd,te->td', act, wd, combine)
        routed = routed.reshape(orig_shape)
        shared = jax.nn.silu(hidden_states @ sg) * (hidden_states @ su) @ sd
        return routed + shared
    x = L0_attn_x
    x = x + 0.5 * _L0_ffn_ref(_layernorm(x, axis=-1), L0_ffn_gate_w, L0_ffn_w_gate, L0_ffn_w_up, L0_ffn_w_down, L0_ffn_sw_gate, L0_ffn_sw_up, L0_ffn_sw_down)
    x = x + _L0_attn_ref(_layernorm(x, axis=-1), L0_attn_ln1_g, L0_attn_ln1_b, L0_attn_ln2_g, L0_attn_ln2_b, L0_attn_tm_decay, L0_attn_tm_first, L0_attn_tm_mk, L0_attn_tm_mv, L0_attn_tm_mr, L0_attn_Wk, L0_attn_Wv, L0_attn_Wr, L0_attn_Wo, L0_attn_cm_mk, L0_attn_cm_mr, L0_attn_Wkey, L0_attn_Wval, L0_attn_Wcr)
    x = x + 0.5 * _L0_ffn_ref(_layernorm(x, axis=-1), L0_ffn_gate_w, L0_ffn_w_gate, L0_ffn_w_up, L0_ffn_w_down, L0_ffn_sw_gate, L0_ffn_sw_up, L0_ffn_sw_down)
    x = x + 0.5 * _L1_ffn_ref(_layernorm(x, axis=-1), L1_ffn_gate_w, L1_ffn_wg, L1_ffn_wu, L1_ffn_wd, L1_ffn_sg, L1_ffn_su, L1_ffn_sd)
    x = x + _L1_attn_ref(_layernorm(x, axis=-1), L1_attn_W_in, L1_attn_b_in, L1_attn_W_out, L1_attn_b_out)
    x = x + 0.5 * _L1_ffn_ref(_layernorm(x, axis=-1), L1_ffn_gate_w, L1_ffn_wg, L1_ffn_wu, L1_ffn_wd, L1_ffn_sg, L1_ffn_su, L1_ffn_sd)
    return x

_drawn_inputs = setup_inputs


def setup_inputs(seed=0):
    import zlib

    import numpy as np

    out = dict(_drawn_inputs(seed))
    spreads = {'L0_attn_ln1_g': (1.0, 0.2),
     'L0_attn_ln1_b': (0.0, 0.278),
     'L0_attn_ln2_g': (1.0, 0.6),
     'L0_attn_ln2_b': (0.0, 0.489),
     'L1_attn_b_in': (0.0, 0.1),
     'L1_attn_b_out': (0.0, 0.465)}
    factors = {'L0_ffn_gate_w': 8.0,
     'L0_ffn_w_gate': 8.0,
     'L0_ffn_w_up': 8.0,
     'L0_ffn_w_down': 8.0,
     'L0_ffn_sw_gate': 3.97,
     'L0_ffn_sw_up': 3.927,
     'L0_ffn_sw_down': 3.916,
     'L1_ffn_gate_w': 8.0,
     'L1_ffn_wg': 8.0,
     'L1_ffn_wu': 8.0,
     'L1_ffn_wd': 8.0,
     'L1_ffn_sg': 8.0,
     'L1_ffn_su': 8.0,
     'L1_ffn_sd': 8.0}
    for name, (base, spread) in spreads.items():
        noise = np.random.default_rng([zlib.crc32(name.encode()), seed]).standard_normal(out[name].shape)
        drawn = base * np.exp(spread * noise) if base else spread * noise
        out[name] = jnp.asarray(drawn.astype(out[name].dtype))
    for name, factor in factors.items():
        out[name] = (out[name] * factor).astype(out[name].dtype)
    return out
```

```python
from contextlib import ExitStack

import concourse.bass as bass
from concourse import mybir

F32 = mybir.dt.float32
F32R = mybir.dt.float32r
ACT = mybir.ActivationFunctionType
ALU = mybir.AluOpType
AX = mybir.AxisListType

P = 128
D = 256
KD = D // P
BATCH, SEQ = 2, 1024
NTOK = BATCH * SEQ
BT = 512
NB = NTOK // BT
QB = SEQ // BT
NT = BT // P
EPS = 1e-5

CW = 3 * D
PW = 2 * D
SLOT = 2 * CW


class Ffn:

    def __init__(self, experts, top, width, shared, first_slot, nslots):
        self.E, self.K = experts, top
        self.per = P // experts
        self.routed = width // self.per
        self.shared = -(-shared // P)
        self.C = self.routed + self.shared
        self.slot = [(first_slot + c) % nslots for c in range(self.C)]


NSLOTS = 26
L0 = Ffn(8, 2, 176, 352, 0, NSLOTS)
L1 = Ffn(32, 6, 96, 192, L0.C, NSLOTS)
assert L1.C == NSLOTS

A0_PIECES = 13
A0_HID = 8
A1_PIECES = 5
A0_AT = L0.C * SLOT
A0_SCRATCH = 23 * SLOT
A1_SLOT0 = 2
A1_EVICTED = 8
A1_AT = L1.slot[A1_SLOT0] * SLOT
A1_SCRATCH = L1.slot[A1_SLOT0 + 4] * SLOT
assert A0_AT + A0_PIECES * 2 * PW <= A0_SCRATCH and A1_PIECES * 2 * PW <= 4 * SLOT

VEC = ["ln1_g", "ln1_b", "ln2_g", "ln2_b", "tm_first", "tm_mk", "tm_mv", "tm_mr", "cm_mk", "cm_mr", "b_out"]
VCOL = {n: KD * i for i, n in enumerate(VEC)}
BIN = KD * len(VEC)
NV = BIN + 8



ROUTE0, ROUTE1 = 9, 9
LN_STEPS = 3
A0_STEPS, A1_STEPS = 21, 12

JOBS = 2 * NB
B_ITEMS = L0.C + A0_HID

def program(nc, x_in, w0, w1, wa0, wa1, gate0, gate1, vecs, cs, ident_in, out):
    place = [32 * -(-nc.sbuf_base // 32)]

    def sb(name, shape, dt, at=None):
        size = 4
        for n in shape[1:]:
            size *= n
        if at is None:
            at = place[0]
            place[0] += 32 * -(-size // 32)
        return nc.alloc_sbuf_tensor_at(name, shape, dt, offset=at)

    with ExitStack() as ctx:
        def sem(name):
            return ctx.enter_context(nc.semaphore(name))

        wbyte = place[0]
        W = sb("W", [P, NSLOTS * SLOT], F32R)
        X = sb("X", [P, NB, KD, BT], F32)
        XN = sb("XN", [P, 4, KD, BT], F32R)
        Cn = sb("Cn", [P, KD, BT], F32)
        tm_at = place[0]
        Tm = sb("Tm", [P, KD, BT], F32)
        sum_hi = sb("sum_hi", [P, BT], F32R)
        sum_lo = sb("sum_lo", [P, BT], F32R, tm_at + 4 * BT)
        s_at = place[0]
        S = sb("S", [P, 2, BT], F32)
        hl_at = place[0]
        HL = sb("HL", [P, 2, 2, BT], F32R)
        rsd = sb("rsd", [P, 2, NT], F32)
        cb_at = place[0]
        CB = sb("CB", [P, BT], F32)
        stage_at = place[0]
        stage = sb("stage", [P, 3 * CW], F32)
        ident = sb("ident", [P, P], F32)
        ones = sb("ones", [P, P], F32R)
        vec = sb("vec", [P, NV], F32)
        g0 = sb("g0", [P, KD, L0.E], F32)
        g1 = sb("g1", [P, KD, L1.E], F32)
        epsv = sb("epsv", [P, 1], F32)
        idle = sb("idle", [P, 2], F32)
        small = sb("small", [P, 2, NT], F32)
        halo = sb("halo", [P, 3, 2, KD], F32)
        apart = sb("apart", [P, QB, KD], F32)
        Acol = sb("Acol", [P, KD], F32)
        assert place[0] <= nc.sbuf_usable_end

        at0, at1 = wbyte + 4 * A0_SCRATCH, wbyte + 4 * A1_SCRATCH
        x_raw = sb("x_raw", [P, NTOK // P, D], F32, at0)
        XA = sb("XA", [P, KD, BT], F32, at0)
        Hb = sb("Hb", [P, KD, BT + 2], F32, at0 + 4096)
        OP = sb("OP", [P, 2, KD, BT], F32R, at0 + 4096 + 4 * KD * (BT + 2) + 16)
        M = sb("M", [P, KD, BT], F32, stage_at)
        Dl = sb("Dl", [P, KD, BT], F32, stage_at + 4096)
        QQ = sb("QQ", [P, QB, KD, BT], F32, at1)
        XR = sb("XR", [P, QB, KD, BT], F32, at1 + 8192)
        CS = sb("CS", [P, 2, BT], F32, at1 + 16384)
        KK = sb("KK", [P, KD, BT], F32, at1 + 20480)

        key_sq = sb("key_sq", [P, KD, BT], F32, hl_at)
        turn = sb("turn", [P, KD, BT], F32, hl_at + 8 * BT)
        ksum_hi = sb("ksum_hi", [P, BT], F32R, cb_at)
        ksum_lo = sb("ksum_lo", [P, BT], F32R, s_at)
        key_norm = sb("key_norm", [P, BT], F32, s_at + 4 * BT)

        ps = ctx.enter_context(nc.psum_tensor("ps", [P, 8, BT], F32))
        YB, GB, AUX = 0, 2, 6

        def chunk_w(f, c, what, part, k):
            a = f.slot[c] * SLOT + part * CW + {"gate": 0, "up": D, "down": 2 * D}[what] + k * P
            return W[:, a:a + P]

        def piece_w(at, i, part, a):
            a = at + i * 2 * PW + part * PW + a
            return W[:, a:a + P]

        def col(name, k):
            return vec[:, VCOL[name] + k:VCOL[name] + k + 1]

        def bcol(m):
            return vec[:, BIN + m:BIN + m + 1]

        def xblock(b):
            return X[:, bass.ds(b, 1)].rearrange("p a k t -> p (a k) t")

        def xn(b, part):
            return XN[:, bass.ds((b % 2) * 2 + part, 1)].rearrange("p a k t -> p (a k) t")

        def both(row):
            return row.unsqueeze(1).broadcast_to([P, KD, BT])

        consts_in = sem("consts_in")
        consts_ready = sem("consts_ready")
        x_landed = sem("x_landed")
        raw_landed = [sem(f"raw_landed{i}") for i in range(3)]
        hi_split = sem("hi_split")
        w_ready = sem("w_ready")
        x_turned = sem("x_turned")
        x_ready = sem("x_ready")
        cs_landed = sem("cs_landed")
        out_turned = sem("out_turned")
        out_copied = sem("out_copied")
        out_sent = sem("out_sent")
        out_free = sem("out_free")

        class Ln:

            def __init__(self, name):
                self.v = sem(name + "_dve")
                self.sum_ready = sem(name + "_sum")
                self.stat = sem(name + "_stat")
                self.centred = sem(name + "_centred")
                self.sq = sem(name + "_sq")
                self.std = sem(name + "_std")
                self.diag = sem(name + "_diag")
                self.xnf = sem(name + "_xnf")
                self.xh = sem(name + "_xh")
                self.xn = sem(name + "_xn")

        lnj = Ln("lnj")
        lni = Ln("lni")

        class FfnSems:

            def __init__(self, name):
                self.gu = sem(name + "_gu")
                self.silu = sem(name + "_silu")
                self.prod = sem(name + "_prod")
                self.gated = sem(name + "_gated")
                self.hi = sem(name + "_hi")
                self.lo = sem(name + "_lo")
                self.down = sem(name + "_down")
                self.logits = sem(name + "_logits")
                self.zed = sem(name + "_zed")
                self.score = sem(name + "_score")
                self.rv = sem(name + "_rv")
                self.rep = sem(name + "_rep")
                self.turned = sem(name + "_turned")
                self.cb = sem(name + "_cb")

        class Attn0Sems:

            def __init__(self, name):
                self.v = sem(name + "_v")
                self.mixed = sem(name + "_mixed")
                self.mix_hi = sem(name + "_mix_hi")
                self.mix_lo = sem(name + "_mix_lo")
                self.proj = sem(name + "_proj")
                self.v2 = sem(name + "_v2")
                self.std2 = sem(name + "_std2")
                self.ww = sem(name + "_ww")
                self.arg = sem(name + "_arg")
                self.e2 = sem(name + "_e2")
                self.sig = sem(name + "_sig")
                self.sr = sem(name + "_sr")

        class Attn1Sems:

            def __init__(self, name):
                self.v = sem(name + "_v")
                self.kvq = sem(name + "_kvq")
                self.xr = sem(name + "_xr")
                self.rot = sem(name + "_rot")
                self.k2 = sem(name + "_k2")
                self.ksq = sem(name + "_ksq")
                self.ksum = sem(name + "_ksum")
                self.kstat = sem(name + "_kstat")
                self.knorm = sem(name + "_knorm")
                self.kv = sem(name + "_kv")
                self.q = sem(name + "_q")
                self.q2 = sem(name + "_q2")
                self.mixed = sem(name + "_mixed")
                self.mix_hi = sem(name + "_mix_hi")
                self.mix_lo = sem(name + "_mix_lo")
                self.y = sem(name + "_y")

        F0, F1, A0, A1 = FfnSems("f0"), FfnSems("f1"), Attn0Sems("a0"), Attn1Sems("a1")
        order1b = [0, 1] + list(range(A1_SLOT0 + A1_EVICTED, L1.C)) + list(range(A1_SLOT0, A1_SLOT0 + A1_EVICTED))
        order0, order1a = list(range(L0.C)), list(range(L1.C))

        LAST0 = (JOBS - 1) * L0.C + NB * A0_HID
        pieces = []
        piece_of = {}

        def piece(key, src, start, n, free=None):
            piece_of[key] = len(pieces)
            pieces.append((src, start, n, free))

        for c in range(L0.C):
            piece(("f0", c), w0[c], L0.slot[c] * SLOT, CW)
        for i in range(A0_PIECES):
            piece(("a0", i), wa0[i], A0_AT + i * 2 * PW, PW)
        for c in range(L1.C):
            free = (x_ready, NB + 2 * NB + 1)
            if L1.slot[c] < L0.C:
                free = (F0.down, LAST0 + L1.slot[c] + 1)
            piece(("f1a", c), w1[c], L1.slot[c] * SLOT, CW, free)
        for i in range(A1_PIECES):
            piece(("a1", i), wa1[i], A1_AT + i * 2 * PW, PW, (F1.down, (NB - 1) * L1.C + A1_SLOT0 + 4))
        for c in range(A1_SLOT0, A1_SLOT0 + A1_EVICTED):
            piece(("f1b", c), w1[c], L1.slot[c] * SLOT, CW, (x_ready, 6 * NB))
        for c in order1b:
            piece_of.setdefault(("f1b", c), piece_of[("f1a", c)])
        block = ctx.enter_context(nc.Block())

        @block.sync
        def _(sp):
            sp.dma_start(x_raw[:], x_in.rearrange("(a p) d -> p a d", p=P)).then_inc(x_landed, 16)
            for dst, src in ((ident, ident_in), (vec, vecs), (g0, gate0), (g1, gate1)):
                sp.dma_start(dst[:], src).then_inc(consts_in, 16)
            for i, (src, start, n, free) in enumerate(pieces):
                if i >= 3:
                    sp.wait_ge(w_ready, i - 2)
                if i == piece_of[("f1a", 0)]:
                    sp.wait_ge(x_ready, NB + 2 * NB + 1)
                a = (i % 3) * CW
                sp.dma_start(stage[:, a:a + n], src).then_inc(raw_landed[i % 3], 16)
                if i == piece_of[("a1", A1_PIECES - 1)]:
                    for b in range(NB):
                        if b == 0:
                            sp.wait_ge(F1.down, (NB - 1) * L1.C + A1_SLOT0 + A1_EVICTED)
                        else:
                            sp.wait_ge(A1.q, b)
                        sp.dma_start(CS[:], cs[b % QB]).then_inc(cs_landed, 16)
            def store(b):
                sp.wait_ge(out_copied, b + 2)
                sp.dma_start(out.rearrange("(b a p) d -> b p a d", b=NB, p=P)[b],
                             stage[:, 0:NT * D].rearrange("p (a d) -> p a d", a=NT)).then_inc(out_sent, 16)
                sp.wait_ge(out_sent, 16 * (b + 1))
                sp.sem_inc(out_free, 1)

            sp.sem_inc(out_free, 1)
            for b in range(NB):
                store(b)
            sp.wait_ge(out_sent, 16 * NB)

        @block.gpsimd
        def _(pool):
            for i, (src, start, n, free) in enumerate(pieces):
                a = (i % 3) * CW
                pool.wait_ge(raw_landed[i % 3], 16 * (i // 3 + 1))
                if free:
                    pool.wait_ge(*free)
                nc.gpsimd.tensor_scalar(W[:, start:start + n], stage[:, a:a + n], 1.0, 0.0, ALU.mult, ALU.add).then_inc(hi_split, 1)
                pool.wait_ge(hi_split, i + 1)
                nc.gpsimd.tensor_tensor(W[:, start + n:start + 2 * n], stage[:, a:a + n],
                                        W[:, start:start + n].bitcast(F32), ALU.subtract).then_inc(w_ready, 1)

        @block.tensor
        def _(pe):
            mm = nc.tensor.matmul

            def product(dst, terms):
                passes = [(l[0], r[0]) for l, r in terms] + [(l[1], r[0]) for l, r in terms] + [(l[0], r[1]) for l, r in terms]
                for n, (l, r) in enumerate(passes):
                    last = mm(dst, l, r, start=(n == 0), stop=(n == len(passes) - 1))
                return last

            def ln_mean(L, r):
                pe.wait_ge(L.sum_ready, r + 1)
                mm(ps[:, AUX + 1, :], ones[:, :], sum_hi[:, :], start=True, stop=False)
                mm(ps[:, AUX + 1, :], ones[:, :], sum_lo[:, :], start=False, stop=True).then_inc(L.stat, 1)

            def ln_squares(L, r):
                pe.wait_ge(L.sq, r + 1)
                for t in range(NT):
                    for k in range(KD):
                        last = mm(ps[:, AUX, t:t + 1], Tm[:, k, t * P:(t + 1) * P], ones[:, 0:1].bitcast(F32), start=(k == 0), stop=(k == KD - 1))
                last.then_inc(L.stat, 1)

            def ln_spread(L, r):
                pe.wait_ge(L.diag, r + 1)
                mm(ps[:, AUX + 1, :], ones[:, :].bitcast(F32), Tm[:, 0, :], start=True, stop=True).then_inc(L.stat, 1)

            pe.wait_ge(x_landed, 16)
            pe.wait_ge(consts_in, 64)
            for b in range(NB):
                if b >= 2:
                    pe.wait_ge(x_ready, b - 1)
                for k in range(KD):
                    for t in range(NT):
                        last = nc.tensor.transpose(ps[:, GB + 2 * (b % 2) + k, t * P:(t + 1) * P],
                                                   x_raw[:, b * NT + t, k * P:(k + 1) * P], ident[:, :])
                last.then_inc(x_turned, 1)
            pe.wait_ge(consts_ready, 1)
            ln_mean(lnj, 0)
            ln_squares(lnj, 0)
            ln_spread(lnj, 0)
            pe.wait_ge(x_ready, NB)

            def up(f, fs, w_of, n, i, r):
                c = w_of[1][i]
                xh, xl = xn(r, 0), xn(r, 1)
                pe.wait_ge(w_ready, piece_of[(w_of[0], c)] + 1)
                if i >= 2:
                    pe.wait_ge(fs.prod, n * f.C + i - 1)
                for u, what in enumerate(("gate", "up")):
                    last = product(ps[:, GB + 2 * (i % 2) + u, :],
                                   [((chunk_w(f, c, what, 0, k), chunk_w(f, c, what, 1, k)), (xh[:, k], xl[:, k]))
                                    for k in range(KD)])
                last.then_inc(fs.gu, 1)

            def head(f, fs, w_of, gw, n, r):
                pe.wait_ge(lnj.xn, r + 1)
                for t in range(NT):
                    for k in range(KD):
                        last = mm(ps[:, AUX + 1, t * f.E:(t + 1) * f.E], Cn[:, k, t * P:(t + 1) * P], gw[:, k, :],
                                  start=(k == 0), stop=(k == KD - 1))
                last.then_inc(fs.logits, 1)
                up(f, fs, w_of, n, 0, r)

            def slot(f, fs, w_of, n, t, r, xr, after, attention=None, final=None):
                C = f.C

                def down(i):
                    c = w_of[1][i]
                    pe.wait_ge(fs.lo, t + i + 1)
                    for part_w, part_h in ((0, 0), (1, 0), (0, 1)):
                        for m in range(KD):
                            last = mm(ps[:, YB + m, :], chunk_w(f, c, "down", part_w, m), HL[:, part_h, i % 2, :],
                                      start=(i == 0 and part_w == part_h), stop=(i == C - 1 and part_h == 1))
                    last.then_inc(fs.down, 1)

                for i in range(1, C):
                    up(f, fs, w_of, n, i, r)
                    if i == 2:
                        pe.wait_ge(fs.rep, n + 1)
                        for tile in range(NT):
                            last = nc.tensor.transpose(ps[:, AUX, tile * P:(tile + 1) * P],
                                                       Cn[:, 0, tile * P:(tile + 1) * P], ident[:, :])
                        last.then_inc(fs.turned, 1)
                    if attention:
                        attention(i)
                    elif i == 5:
                        pe.wait_ge(fs.cb, n + 1)
                        ln_mean(lnj, r + 1)
                    elif i == 7:
                        ln_squares(lnj, r + 1)
                    elif i == 9:
                        ln_spread(lnj, r + 1)
                    if i == 3:
                        pe.wait_ge(x_ready, xr)
                        if final:
                            pe.wait_ge(out_copied, n - NB + 1)
                    if i >= 3:
                        down(i - 3)
                down(C - 3)
                if attention:
                    attention("ahead of the last two products")
                down(C - 2)
                if attention:
                    down(C - 1)
                    attention("channel mixing")
                else:
                    if after:
                        after()
                    down(C - 1)
                if final:
                    pe.wait_ge(x_ready, xr + 1)
                    for tile in range(NT):
                        for k in range(KD):
                            a = (tile % 2) * D + k * P
                            last = nc.tensor.transpose(ps[:, YB + tile // 2, a:a + P], Tm[:, k, tile * P:(tile + 1) * P], ident[:, :])
                    last.then_inc(out_turned, 1)

            def attn0(ph, fs, n, t, r, xr, after):
                b = n - 1
                mixed0 = [(OP[:, 0, k, :], OP[:, 1, k, :]) for k in range(KD)]
                other = r + 1
                mixed1 = [(xn(other, 0)[:, k], xn(other, 1)[:, k]) for k in range(KD)]

                def project(piece, i, op):
                    pe.wait_ge(ph.mix_lo, b * 6 + i + 1)
                    for m in range(KD):
                        a = lambda k: k * D + m * P
                        last = product(ps[:, AUX + m, :],
                                       [((piece_w(A0_AT, piece, 0, a(k)), piece_w(A0_AT, piece, 1, a(k))), op[k]) for k in range(KD)])
                    last.then_inc(ph.proj, 1)

                def hidden(h):
                    if h >= 2:
                        pe.wait_ge(fs.silu, t + L0.C + h - 1)
                    product(ps[:, GB + 2 * (h % 2), :],
                            [((piece_w(A0_AT, 5 + h, 0, k * P), piece_w(A0_AT, 5 + h, 1, k * P)), mixed0[k])
                             for k in range(KD)]).then_inc(fs.gu, 1)

                def down(h):
                    pe.wait_ge(fs.lo, t + L0.C + h + 1)
                    for part_w, part_h in ((0, 0), (1, 0), (0, 1)):
                        for m in range(KD):
                            last = mm(ps[:, YB + m, :], piece_w(A0_AT, 5 + h, part_w, D + m * P), HL[:, part_h, h % 2, :],
                                      start=(h == 0 and part_w == part_h), stop=(h == A0_HID - 1 and part_h == 1))
                    last.then_inc(fs.down, 1)

                def do(i):
                    if i == 2:
                        ln_mean(lni, 2 * b)
                    if i == 3:
                        pe.wait_ge(fs.cb, n + 1)
                        ln_squares(lni, 2 * b)
                    if i == 4:
                        pe.wait_ge(lni.diag, 2 * b + 1)
                        mm(ps[:, AUX, :], ones[:, :].bitcast(F32), Tm[:, 0, :], start=True, stop=True)
                        mm(ps[:, AUX + 1, :], ones[:, :].bitcast(F32), Tm[:, 1, :], start=True, stop=True).then_inc(lni.stat, 1)
                    if i == 7:
                        pe.wait_ge(w_ready, piece_of[("a0", A0_PIECES - 1)] + 1)
                        project(0, 0, mixed0)
                    if i == 8:
                        pe.wait_ge(ph.ww, b + 1)
                        project(2, 1, mixed1)
                    if i == 9:
                        pe.wait_ge(ph.sig, b + 1)
                        project(1, 2, mixed0)
                    if i == 11:
                        project(3, 3, mixed1)
                    if i == 12:
                        ln_mean(lni, 2 * b + 1)
                    if i == 13:
                        ln_squares(lni, 2 * b + 1)
                    if i == "ahead of the last two products":
                        ln_spread(lni, 2 * b + 1)
                    if i == "channel mixing":
                        pe.wait_ge(ph.mix_lo, b * 6 + 5)
                        for h in range(A0_HID):
                            hidden(h)
                            if h == 2:
                                project(4, 5, mixed1)
                                pe.wait_ge(x_ready, xr + 1)
                            if h == 3:
                                pe.wait_ge(ph.sr, b + 1)
                                ln_mean(lnj, r + 1)
                            if h == 5:
                                ln_squares(lnj, r + 1)
                            if h == 6:
                                ln_spread(lnj, r + 1)
                            if h >= 3:
                                down(h - 3)
                        down(A0_HID - 3)
                        down(A0_HID - 2)
                        after()
                        down(A0_HID - 1)
                return do

            def attn1(ph):
                with pe.Fori(0, BATCH) as s:
                    for q in range(QB):
                        b = s * QB + q
                        r = JOBS + NB + b
                        if q == 0:
                            pe.wait_ge(w_ready, piece_of[("a1", A1_PIECES - 1)] + 1)
                        pe.wait_ge(lnj.xn, r + 1)
                        op = [(XN[:, 2 * (q % 2), k, :], XN[:, 2 * (q % 2) + 1, k, :]) for k in range(KD)]
                        for m, bank in enumerate((2, 3, 4, 5, 0, 1, 2, 3)):
                            if m == 0 and q == 0:
                                pe.wait_ge(x_ready, 5 * NB + b)
                            if m == 0 and q == 1:
                                pe.wait_ge(ph.q, b)
                                pe.wait_ge(ph.q2, b)
                            if m == 6:
                                pe.wait_ge(ph.rot, b + 1)
                            product(ps[:, bank, :],
                                    [((piece_w(A1_AT, m // 2, 0, k * D + (m % 2) * P), piece_w(A1_AT, m // 2, 1, k * D + (m % 2) * P)), op[k])
                                     for k in range(KD)]).then_inc(ph.kvq, 1)
                            if m == 5:
                                ln_mean(lnj, r + 1)
                        pe.wait_ge(ph.ksum, b + 1)
                        mm(ps[:, AUX, :], ones[:, :], ksum_hi[:, :], start=True, stop=False)
                        mm(ps[:, AUX, :], ones[:, :], ksum_lo[:, :], start=False, stop=True).then_inc(ph.kstat, 1)
                        pe.wait_ge(ph.knorm, b + 1)
                        ln_squares(lnj, r + 1)
                        ln_spread(lnj, r + 1)
                    for q in range(QB):
                        b = s * QB + q
                        pe.wait_ge(ph.mix_lo, b + 1)
                        if q == 1:
                            pe.wait_ge(x_ready, 5 * NB + b)
                        for m in range(KD):
                            last = product(ps[:, YB + m, :],
                                           [((piece_w(A1_AT, 4, 0, k * D + m * P), piece_w(A1_AT, 4, 1, k * D + m * P)),
                                             (HL[:, 0, k, :], HL[:, 1, k, :])) for k in range(KD)])
                        last.then_inc(ph.y, 1)

            g0job = lambda n: lambda: head(L0, F0, ("f0", order0), g0, n, n)
            g0job(0)()
            slot(L0, F0, ("f0", order0), 0, 0, 0, NB, g0job(1))
            with pe.Fori(1, NB + 1) as n:
                t, xr = L0.C + (n - 1) * B_ITEMS, NB + 2 * n - 1
                slot(L0, F0, ("f0", order0), n, t, n, xr, None, attn0(A0, F0, n, t, n, xr, g0job(n + 1)))
            with pe.Fori(NB + 1, JOBS - 1) as n:
                slot(L0, F0, ("f0", order0), n, n * L0.C + NB * A0_HID, n, 2 * NB + n, g0job(n + 1))
            g1job = lambda key, order, n, r: lambda: head(L1, F1, (key, order), g1, n, r)
            n = JOBS - 1
            slot(L0, F0, ("f0", order0), n, LAST0, n, 2 * NB + n, g1job("f1a", order1a, 0, JOBS))
            with pe.Fori(0, NB - 1) as n:
                slot(L1, F1, ("f1a", order1a), n, n * L1.C, JOBS + n, 4 * NB + n, g1job("f1a", order1a, n + 1, JOBS + n + 1))
            n = NB - 1
            slot(L1, F1, ("f1a", order1a), n, n * L1.C, JOBS + n, 4 * NB + n, None)
            attn1(A1)
            g1job("f1b", order1b, NB, JOBS + 2 * NB)()
            with pe.Fori(NB, JOBS - 1) as n:
                slot(L1, F1, ("f1b", order1b), n, n * L1.C, JOBS + NB + n, 5 * NB + n, g1job("f1b", order1b, n + 1, JOBS + NB + n + 1), final=True)
            n = JOBS - 1
            slot(L1, F1, ("f1b", order1b), n, n * L1.C, JOBS + NB + n, 5 * NB + n, None, final=True)

        @block.scalar
        def _(act):
            fn = nc.scalar.activation

            def ln_sq(L, r):
                act.wait_ge(L.centred, r + 1)
                fn(Tm[:, :, :], Cn[:, :, :], ACT.Square).then_inc(L.sq, 1)

            def ln_std(L, r):
                act.wait_ge(L.stat, 3 * r + 2)
                fn(rsd[:, 0, :], ps[:, AUX, 0:NT], ACT.Sqrt, bias=epsv[:, :]).then_inc(L.std, 1)

            def ln_xh(r, par):
                act.wait_ge(lnj.xnf, r + 1)
                fn(idle[:, 1:2], epsv[:, :], ACT.Copy)
                fn(xn(par, 0), Cn[:, :, :], ACT.Copy).then_inc(lnj.xh, 1)

            act.sem_inc(out_copied, 1)
            act.wait_ge(consts_ready, 1)
            ln_sq(lnj, 0)
            ln_std(lnj, 0)
            ln_xh(0, 0)

            def copy_out(b):
                act.wait_ge(out_turned, b + 1)
                act.wait_ge(out_free, b + 1)
                fn(stage[:, 0:NT * D], ps[:, YB:YB + 2, :], ACT.Copy).then_inc(out_copied, 1)

            def score(f, fs, n):
                scores = Cn[:, 1, 0:NT * (f.E + 8)].rearrange("p (t e) -> p t e", t=NT)
                if f is L0:
                    act.wait_ge(fs.zed, n + 1)
                    fn(scores[:, :, 0:f.E], scores[:, :, 0:f.E], ACT.Exp).then_inc(fs.score, 1)
                else:
                    act.wait_ge(fs.logits, n + 1)
                    fn(scores[:, :, 0:f.E], ps[:, AUX + 1, 0:NT * f.E].rearrange("p (t e) -> p t e", t=NT),
                       ACT.Sigmoid).then_inc(fs.score, 1)

            def slot(f, fs, n, t, r, after, attention=None, final=False):
                C = f.C

                def turned():
                    act.wait_ge(fs.turned, n + 1)
                    fn(CB[:, :], ps[:, AUX, :], ACT.Copy).then_inc(fs.cb, 1)

                def lead_hidden(i):
                    if i < f.shared:
                        act.wait_ge(fs.prod, n * C + i + 1)
                    else:
                        act.wait_ge(fs.gated, n * f.routed + i - f.shared + 1)
                    hidden_hi(fs, t + i, i % 2)

                for i in range(C):
                    silu(fs, t + i, i % 2)
                    if i == 2:
                        turned()
                    if attention and i > 0:
                        attention(i - 1, late=True)
                    if i > 0:
                        lead_hidden(i - 1)
                    if attention:
                        attention(i)
                    elif i == 5:
                        ln_sq(lnj, r + 1)
                    elif i == 7:
                        ln_std(lnj, r + 1)
                    elif i == 10:
                        ln_xh(r + 1, r + 1)
                lead_hidden(C - 1)
                if attention:
                    attention(C)
                if after:
                    after()
                if final:
                    copy_out(n - NB)

            def silu(fs, t, half):
                act.wait_ge(fs.gu, t + 1)
                if not isinstance(t, int) or t > 1:
                    act.wait_ge(fs.lo, t - 1)
                fn(S[:, half, :], ps[:, GB + 2 * half, :], ACT.Silu).then_inc(fs.silu, 1)

            def hidden_hi(fs, t, half):
                if not isinstance(t, int) or t > 1:
                    act.wait_ge(fs.down, t - 1)
                fn(HL[:, 0, half, :], S[:, half, :], ACT.Copy).then_inc(fs.hi, 1)

            def attn0(ph, fs, n, t, r):
                b = n - 1

                def lead(i, buf):
                    act.wait_ge(ph.mixed, b * 6 + i + 1)
                    if buf:
                        fn(idle[:, 1:2], epsv[:, :], ACT.Copy)
                    fn(OP[:, 0] if buf == 0 else xn(r + 1, 0), M[:, :, :], ACT.Copy).then_inc(ph.mix_hi, 1)

                def do(i, late=False):
                    if late:
                        if i == 5:
                            lead(0, 0)
                        if i == 6:
                            lead(1, 1)
                        if i == 7:
                            lead(2, 0)
                        if i == 9:
                            lead(3, 1)
                        return
                    if i == 2:
                        ln_sq(lni, 2 * b)
                    if i == 3:
                        ln_std(lni, 2 * b)
                        act.wait_ge(ph.v2, b + 1)
                        fn(small[:, 1, :], small[:, 0, :], ACT.Sqrt, bias=epsv[:, :]).then_inc(ph.std2, 1)
                    if i == 7:
                        act.wait_ge(ph.proj, b * 5 + 1)
                        for k in range(KD):
                            last = fn(Cn[:, k, :], ps[:, AUX + k, :], ACT.Identity, bias=col("tm_first", k))
                        last.then_inc(ph.ww, 1)
                    if i == 8:
                        act.wait_ge(ph.proj, b * 5 + 2)
                        fn(Dl[:, :, :], ps[:, AUX:AUX + 2, :], ACT.Sigmoid).then_inc(ph.sig, 1)
                        act.wait_ge(ph.arg, b + 1)
                        fn(Tm[:, :, :], Cn[:, :, :], ACT.Exp)
                        fn(Cn[:, :, :], Cn[:, :, :], ACT.Exp, scale=-1.0).then_inc(ph.e2, 1)
                    if i == 12:
                        ln_sq(lni, 2 * b + 1)
                    if i == 13:
                        ln_std(lni, 2 * b + 1)
                    if i == L0.C:
                        lead(4, 0)
                        lead(5, 1)
                        for h in range(A0_HID):
                            silu(fs, t + L0.C + h, h % 2)
                            if h > 0:
                                act.wait_ge(fs.silu, t + L0.C + h)
                                hidden_hi(fs, t + L0.C + h - 1, (h - 1) % 2)
                            if h == 2:
                                act.wait_ge(ph.proj, b * 5 + 5)
                                fn(Dl[:, :, :], ps[:, AUX:AUX + 2, :], ACT.Sigmoid).then_inc(ph.sr, 1)
                            if h == 3:
                                ln_sq(lnj, r + 1)
                            if h == 5:
                                ln_std(lnj, r + 1)
                            if h == 6:
                                ln_xh(r + 1, r + 1)
                        act.wait_ge(fs.silu, t + B_ITEMS)
                        hidden_hi(fs, t + L0.C + A0_HID - 1, 1)
                return do

            def attn1(ph):
                with act.Fori(0, BATCH) as s:
                    for q in range(QB):
                        b = s * QB + q
                        r = JOBS + NB + b
                        if q == 0:
                            act.wait_ge(x_ready, 5 * NB + b)
                            act.wait_ge(lnj.xn, r + 1)
                        fn(XR[:, q], Cn[:, :, :], ACT.Copy).then_inc(ph.xr, 1)
                        act.wait_ge(ph.kvq, 8 * b + 3)
                        if q == 1:
                            act.wait_ge(ph.v, b * A1_STEPS)
                        fn(KK[:, 1, :], ps[:, 4, :], ACT.Identity, bias=bcol(2)).then_inc(ph.k2, 1)
                        act.wait_ge(ph.rot, b + 1)
                        act.wait_ge(ph.k2, b + 1)
                        fn(key_sq[:, 0, :], KK[:, 0, :], ACT.Square)
                        fn(key_sq[:, 1, :], KK[:, 1, :], ACT.Square).then_inc(ph.ksq, 1)
                        ln_sq(lnj, r + 1)
                        act.wait_ge(ph.kstat, b + 1)
                        fn(key_norm[:, :], ps[:, AUX, :], ACT.Sqrt, scale=float(D)).then_inc(ph.knorm, 1)
                        act.wait_ge(ph.kvq, 8 * b + 8)
                        fn(QQ[:, q, 1, :], ps[:, 3, :], ACT.Identity, bias=bcol(7)).then_inc(ph.q2, 1)
                        ln_std(lnj, r + 1)
                        ln_xh(r + 1, q + 1)
                    for q in range(QB):
                        b = s * QB + q
                        act.wait_ge(ph.mixed, b + 1)
                        if q == 1:
                            act.wait_ge(ph.y, b)
                        fn(HL[:, 0, :, :], (KK, Tm)[q][:, :, :], ACT.Copy).then_inc(ph.mix_hi, 1)

            score0 = lambda n: lambda: score(L0, F0, n)
            score1 = lambda n: lambda: score(L1, F1, n)
            score0(0)()
            slot(L0, F0, 0, 0, 0, score0(1))
            with act.Fori(1, NB + 1) as n:
                t = L0.C + (n - 1) * B_ITEMS
                slot(L0, F0, n, t, n, score0(n + 1), attn0(A0, F0, n, t, n))
            with act.Fori(NB + 1, JOBS - 1) as n:
                slot(L0, F0, n, n * L0.C + NB * A0_HID, n, score0(n + 1))
            n = JOBS - 1
            slot(L0, F0, n, LAST0, n, score1(0))
            act.wait_ge(F0.lo, LAST0 + L0.C)
            slot(L1, F1, 0, 0, JOBS, score1(1))
            with act.Fori(1, NB - 1) as n:
                slot(L1, F1, n, n * L1.C, JOBS + n, score1(n + 1))
            n = NB - 1
            slot(L1, F1, n, n * L1.C, JOBS + n, None)
            attn1(A1)
            score1(NB)()
            with act.Fori(NB, JOBS - 1) as n:
                slot(L1, F1, n, n * L1.C, JOBS + NB + n, score1(n + 1), final=True)
            n = JOBS - 1
            slot(L1, F1, n, n * L1.C, JOBS + NB + n, None, final=True)

        @block.vector
        def _(dve):
            tt, ts, stt, copy = nc.vector.tensor_tensor, nc.vector.tensor_scalar, nc.vector.scalar_tensor_tensor, nc.vector.tensor_copy

            class Steps:

                def __init__(self, s, base):
                    self.s, self.base, self.n = s, base, 0

                def do(self, ins):
                    self.n += 1
                    ins.then_inc(self.s, 1)

                def sync(self):
                    dve.wait_ge(self.s, self.base + self.n)

            def ln_sum(L, r, src):
                st = Steps(L.v, LN_STEPS * r)
                st.do(tt(Tm[:, 0, :], src[:, 0], src[:, 1], ALU.add))
                st.sync()
                st.do(copy(sum_hi[:, :], Tm[:, 0, :]))
                st.sync()
                tt(sum_lo[:, :], Tm[:, 0, :], sum_hi[:, :].bitcast(F32), ALU.subtract).then_inc(L.sum_ready, 1)

            def ln_centre(L, r, src):
                dve.wait_ge(L.stat, 3 * r + 1)
                tt(Cn[:, :, :], src, both(ps[:, AUX + 1, :]), ALU.subtract).then_inc(L.centred, 1)

            def ln_diag(L, r):
                st = Steps(L.v, LN_STEPS * r)
                st.n = 2
                dve.wait_ge(L.std, r + 1)
                st.do(nc.vector.reciprocal(rsd[:, 1, :], rsd[:, 0, :]))
                st.sync()
                stt(Tm[:, 0, :].rearrange("p (t j) -> p t j", t=NT), ident[:, :].unsqueeze(1).broadcast_to([P, NT, P]), float(D),
                    rsd[:, 1, :].unsqueeze(2).broadcast_to([P, NT, P]), ALU.mult, ALU.mult).then_inc(L.diag, 1)

            def ln_norm(L, r, dst):
                dve.wait_ge(L.stat, 3 * r + 3)
                tt(dst, Cn[:, :, :], both(ps[:, AUX + 1, :]), ALU.mult).then_inc(L.xnf, 1)

            def ln_xl(r, par):
                dve.wait_ge(lnj.xh, r + 1)
                tt(xn(par, 1), Cn[:, :, :], xn(par, 0).bitcast(F32), ALU.subtract).then_inc(lnj.xn, 1)

            dve.wait_ge(consts_in, 64)
            nc.vector.memset(epsv[:, :], EPS)
            nc.vector.memset(halo[:, :, :, :], 0.0)
            nc.vector.memset(ones[:, :].bitcast(F32), 1.0 / D).then_inc(consts_ready, 1)
            for b in range(NB):
                dve.wait_ge(x_turned, b + 1)
                copy(X[:, b], ps[:, GB + 2 * (b % 2):GB + 2 * (b % 2) + 2, :]).then_inc(x_ready, 1)
                if b == 1:
                    dve.wait_ge(x_ready, 1)
                    ln_sum(lnj, 0, X[:, 0])
                    ln_centre(lnj, 0, X[:, 0])
                    ln_diag(lnj, 0)
                    ln_norm(lnj, 0, Cn[:, :, :])
                    ln_xl(0, 0)

            def route(ph, f, b):
                E, K, W8 = f.E, f.K, f.E + 8
                scores = Cn[:, 1, 0:NT * W8].rearrange("p (t e) -> p t e", t=NT)
                rest = Cn[:, 1, NT * W8:2 * NT * W8].rearrange("p (t e) -> p t e", t=NT)
                top8 = Cn[:, 1, 2 * NT * W8:2 * NT * W8 + 8 * NT].rearrange("p (t e) -> p t e", t=NT)
                rep = Cn[:, 0, :].rearrange("p (t e r) -> p t e r", t=NT, e=E)
                logits = ps[:, AUX + 1, 0:NT * E].rearrange("p (t e) -> p t e", t=NT)
                over = lambda v: v.unsqueeze(2).broadcast_to([P, NT, E])
                s, c = small[:, 0, :], small[:, 1, :]
                st = Steps(ph.rv, b * (ROUTE0 if f is L0 else ROUTE1))
                dve.wait_ge(ph.logits, b + 1)
                st.do(nc.vector.memset(scores[:, :, E:W8], -1.0))
                if f is L0:
                    st.do(nc.vector.tensor_reduce(s, logits, AX.X, ALU.max))
                    st.sync()
                    tt(scores[:, :, 0:E], logits, over(s), ALU.subtract).then_inc(ph.zed, 1)
                    dve.wait_ge(ph.score, b + 1)
                    st.do(nc.vector.tensor_reduce(s, scores[:, :, 0:E], AX.X, ALU.add))
                    st.sync()
                    st.do(nc.vector.reciprocal(c, s))
                    st.sync()
                    st.do(tt(scores[:, :, 0:E], scores[:, :, 0:E], over(c), ALU.mult))
                else:
                    dve.wait_ge(ph.score, b + 1)
                st.sync()
                nc.vector.memset(idle[:, 0:1], 0.0)
                for t in range(NT):
                    last = nc.vector.max(top8[:, t, :], scores[:, t, :])
                st.do(last)
                st.sync()
                if f is L1:
                    st.do(nc.vector.tensor_reduce(s, top8[:, :, 0:K], AX.X, ALU.add))
                    st.sync()
                    st.do(nc.vector.tensor_scalar(s, s, 1e-20, None, ALU.add))
                    st.sync()
                    st.do(nc.vector.reciprocal(c, s))
                st.do(nc.vector.memset(top8[:, :, K:8], -1.0))
                st.sync()
                nc.vector.memset(idle[:, 0:1], 0.0)
                for t in range(NT):
                    last = nc.vector.match_replace(rest[:, t, :], top8[:, t, :], scores[:, t, :], 0.0)
                st.do(last)
                st.sync()
                st.do(tt(rest[:, :, 0:E], scores[:, :, 0:E], rest[:, :, 0:E], ALU.subtract))
                st.sync()
                if f is L1:
                    st.do(tt(rest[:, :, 0:E], rest[:, :, 0:E], over(c), ALU.mult))
                    st.sync()
                copy(rep, rest[:, :, 0:E].unsqueeze(3).broadcast_to([P, NT, E, f.per])).then_inc(ph.rep, 1)
                assert st.n == (ROUTE0 if f is L0 else ROUTE1), st.n

            def slot(f, fs, n, t, r, xr, after, attention=None, final=False):
                C = f.C
                here, nxt = xblock(n % NB), xblock((n + 1) % NB)
                for i in range(C):
                    dve.wait_ge(fs.silu, t + i + 1)
                    rows = S[:, i % 2, :]
                    tt(rows, rows, ps[:, GB + 2 * (i % 2) + 1, :], ALU.mult).then_inc(fs.prod, 1)
                    if i >= f.shared:
                        if i == f.shared:
                            dve.wait_ge(fs.cb, n + 1)
                        dve.wait_ge(fs.prod, n * C + i + 1)
                        tt(rows, rows, CB[:, :], ALU.mult).then_inc(fs.gated, 1)
                    if attention:
                        attention(i)
                    if i > 0:
                        remainder(fs, t + i - 1, (i - 1) % 2)
                    if attention:
                        pass
                    elif i == 3:
                        dve.wait_ge(x_ready, xr)
                        ln_sum(lnj, r + 1, nxt)
                    elif i == 5:
                        ln_centre(lnj, r + 1, nxt)
                    elif i == 7:
                        ln_diag(lnj, r + 1)
                    elif i == 9:
                        ln_norm(lnj, r + 1, Cn[:, :, :])
                    elif i == 10:
                        ln_xl(r + 1, r + 1)
                remainder(fs, t + C - 1, (C - 1) % 2)
                if after and not attention:
                    after()

                def finish():
                    dve.wait_ge(fs.down, t + C)
                    stt(Tm[:, :, :] if final else here, ps[:, YB:YB + 2, :], 0.5, here, ALU.mult, ALU.add).then_inc(x_ready, 1)

                if attention:
                    attention(C, finish)
                else:
                    finish()

            def remainder(fs, t, half):
                dve.wait_ge(fs.hi, t + 1)
                tt(HL[:, 1, half, :], S[:, half, :], HL[:, 0, half, :].bitcast(F32), ALU.subtract).then_inc(fs.lo, 1)

            def attn0(ph, fs, n, t, r, xr, after):
                b = n - 1
                st = Steps(ph.v, b * A0_STEPS)
                src, nxt = xblock(b), xblock((n + 1) % NB)
                prev, cur = Hb[:, :, 0:BT], Hb[:, :, 1:BT + 1]

                def column(at, which):
                    return halo[:, bass.ds(at, 1), which, :].rearrange("p a k -> p k a")

                def shifted(which, gain, shift):
                    dve.wait_ge(lni.xnf, 2 * b + which + 1)
                    for k in range(KD):
                        st.do(ts(Hb[:, k, 1:BT + 1], Cn[:, k, :], col(gain, k), col(shift, k), ALU.mult, ALU.add))
                    st.do(copy(Hb[:, :, 0:1], column(b % 2, which)))
                    st.sync()
                    st.do(tt(Dl[:, :, :], cur, prev, ALU.subtract))
                    st.do(copy(column(b % 2 + 1, which), Hb[:, :, BT:BT + 1]))
                    st.sync()

                def mix(name):
                    for k in range(KD):
                        last = stt(M[:, k, :], Dl[:, k, :], col(name, k), Hb[:, k, 0:BT], ALU.mult, ALU.add)
                    last.then_inc(ph.mixed, 1)

                def split(i, hi, lo):
                    dve.wait_ge(ph.mix_hi, b * 6 + i + 1)
                    tt(lo, M[:, :, :], hi.bitcast(F32), ALU.subtract).then_inc(ph.mix_lo, 1)
                    dve.wait_ge(ph.mix_lo, b * 6 + i + 1)

                mixed0, mixed1 = (OP[:, 0], OP[:, 1]), (xn(r + 1, 0), xn(r + 1, 1))

                def diagonal(dst, column):
                    return stt(dst.rearrange("p (t j) -> p t j", t=NT), ident[:, :].unsqueeze(1).broadcast_to([P, NT, P]), float(D),
                               column.unsqueeze(2).broadcast_to([P, NT, P]), ALU.mult, ALU.mult)

                def do(i, finish=None):
                    if i == 0:
                        dve.wait_ge(x_ready, xr)
                        ln_sum(lni, 2 * b, src)
                    if i == 2:
                        ln_centre(lni, 2 * b, src)
                    if i == 3:
                        inverse, v2 = rsd[:, 1, :], small[:, 0, :]
                        dve.wait_ge(lni.std, 2 * b + 1)
                        norm = Steps(lni.v, LN_STEPS * 2 * b)
                        norm.n = 2
                        norm.do(nc.vector.reciprocal(inverse, rsd[:, 0, :]))
                        norm.sync()
                        st.do(tt(v2, inverse, ps[:, AUX, 0:NT], ALU.mult))
                        st.sync()
                        tt(v2, v2, inverse, ALU.mult).then_inc(ph.v2, 1)
                        dve.wait_ge(lni.stat, 2 * b * 3 + 2)
                        st.do(diagonal(Tm[:, 0, :], inverse))
                        both_inverse = small[:, 0, :]
                        dve.wait_ge(ph.std2, b + 1)
                        st.do(nc.vector.reciprocal(small[:, 1, :], small[:, 1, :]))
                        st.sync()
                        st.do(tt(both_inverse, small[:, 1, :], inverse, ALU.mult))
                        st.sync()
                        diagonal(Tm[:, 1, :], both_inverse).then_inc(lni.diag, 1)
                    if i == 4:
                        dve.wait_ge(lni.stat, 2 * b * 3 + 3)
                        dve.wait_ge(w_ready, piece_of[("a0", A0_PIECES - 1)] + 1)
                        st.do(tt(XA[:, :, :], Cn[:, :, :], both(ps[:, AUX, :]), ALU.mult))
                        st.sync()
                        ln_norm(lni, 2 * b, Cn[:, :, :])
                    if i == 5:
                        shifted(0, "ln1_g", "ln1_b")
                        mix("tm_mk")
                    if i == 6:
                        split(0, *mixed0)
                        mix("tm_mr")
                    if i == 7:
                        split(1, *mixed1)
                        mix("tm_mv")
                    if i == 8:
                        dve.wait_ge(ph.ww, b + 1)
                        st.do(ts(Tm[:, :, :], Cn[:, :, :], -1e38, None, ALU.max))
                        st.sync()
                        tt(Cn[:, :, :], Cn[:, :, :], Tm[:, :, :], ALU.subtract).then_inc(ph.arg, 1)
                        split(2, *mixed0)
                    if i == 9:
                        dve.wait_ge(ph.proj, b * 5 + 3)
                        dve.wait_ge(ph.e2, b + 1)
                        st.do(tt(Tm[:, :, :], Tm[:, :, :], ps[:, AUX:AUX + 2, :], ALU.mult))
                        st.sync()
                        st.do(tt(Tm[:, :, :], Tm[:, :, :], Cn[:, :, :], ALU.mult))
                        st.sync()
                        tt(M[:, :, :], Dl[:, :, :], Tm[:, :, :], ALU.mult).then_inc(ph.mixed, 1)
                    if i == 10:
                        split(3, *mixed1)
                    if i == 11:
                        dve.wait_ge(ph.proj, b * 5 + 4)
                        st.do(tt(XA[:, :, :], XA[:, :, :], ps[:, AUX:AUX + 2, :], ALU.add))
                        st.sync()
                        ln_sum(lni, 2 * b + 1, XA)
                    if i == 12:
                        ln_centre(lni, 2 * b + 1, XA[:, :, :])
                    if i == 13:
                        ln_diag(lni, 2 * b + 1)
                    if i == L0.C:
                        ln_norm(lni, 2 * b + 1, Cn[:, :, :])
                        shifted(1, "ln2_g", "ln2_b")
                        mix("cm_mk")
                        finish()
                        split(4, *mixed0)
                        mix("cm_mr")
                        ln_sum(lnj, r + 1, nxt)
                        split(5, *mixed1)
                        for h in range(A0_HID):
                            if h > 0:
                                remainder(fs, t + L0.C + h - 1, (h - 1) % 2)
                            if h == 3:
                                ln_centre(lnj, r + 1, nxt)
                            if h == 4:
                                st.do(tt(src, src, XA[:, :, :], ALU.add))
                            if h == 5:
                                ln_diag(lnj, r + 1)
                            if h == 6:
                                ln_norm(lnj, r + 1, Cn[:, :, :])
                            if h == 7:
                                ln_xl(r + 1, r + 1)
                        remainder(fs, t + L0.C + A0_HID - 1, 1)
                        after()
                        dve.wait_ge(fs.down, t + B_ITEMS)
                        dve.wait_ge(ph.sr, b + 1)
                        st.do(tt(Dl[:, :, :], Dl[:, :, :], ps[:, YB:YB + 2, :], ALU.mult))
                        st.sync()
                        tt(src, src, Dl[:, :, :], ALU.add).then_inc(x_ready, 1)
                        assert st.n == A0_STEPS, st.n
                return do

            def attn1(ph):
                with dve.Fori(0, BATCH) as s:
                    for q in range(QB):
                        b = s * QB + q
                        r = JOBS + NB + b
                        st = Steps(ph.v, b * A1_STEPS)
                        nxt = xblock((b + 1) % NB)

                        def rotate(dst, m, bank_a, bank_b):
                            st.do(stt(turn[:, 0, :], ps[:, bank_a, :], bcol(m), CS[:, 0, :], ALU.add, ALU.mult))
                            st.do(stt(turn[:, 1, :], ps[:, bank_b, :], bcol(m + 1), CS[:, 1, :], ALU.add, ALU.mult))
                            st.sync()
                            return tt(dst, turn[:, 0, :], turn[:, 1, :], ALU.add)

                        dve.wait_ge(cs_landed, 16 * (b + 1))
                        dve.wait_ge(ph.kvq, 8 * b + 2)
                        rotate(KK[:, 0, :], 0, 2, 3).then_inc(ph.rot, 1)
                        dve.wait_ge(x_ready, 5 * NB + s * QB)
                        ln_sum(lnj, r + 1, nxt)
                        dve.wait_ge(ph.ksq, b + 1)
                        st.do(tt(key_norm[:, :], key_sq[:, 0, :], key_sq[:, 1, :], ALU.add))
                        st.sync()
                        st.do(copy(ksum_hi[:, :], key_norm[:, :]))
                        st.sync()
                        tt(ksum_lo[:, :], key_norm[:, :], ksum_hi[:, :].bitcast(F32), ALU.subtract).then_inc(ph.ksum, 1)
                        dve.wait_ge(ph.xr, b + 1)
                        ln_centre(lnj, r + 1, nxt)
                        dve.wait_ge(ph.kvq, 8 * b + 7)
                        rotate(QQ[:, q, 0, :], 5, 1, 2).then_inc(ph.q, 1)
                        for k in range(KD):
                            st.do(stt(KK[:, k, :], ps[:, (5, 0)[k], :], bcol(3 + k), KK[:, k, :], ALU.add, ALU.mult))
                        ln_diag(lnj, r + 1)
                        dve.wait_ge(ph.knorm, b + 1)
                        st.do(ts(key_norm[:, :], key_norm[:, :], 1e-12, None, ALU.max))
                        st.sync()
                        st.do(nc.vector.reciprocal(key_norm[:, :], key_norm[:, :]))
                        ln_norm(lnj, r + 1, Cn[:, :, :])
                        st.sync()
                        for k in range(KD):
                            st.do(stt(KK[:, k, :], KK[:, k, :], 1.0, key_norm[:, :], ALU.mult, ALU.mult,
                                      accum_out=apart[:, q, k:k + 1]))
                        ln_xl(r + 1, q + 1)
                        st.sync()
                        dve.wait_ge(ph.q, b + 1)
                        assert st.n == A1_STEPS, st.n
                    st = Steps(ph.kv, s * (1 + 2 * QB))
                    st.do(tt(Acol[:, :], apart[:, 0, :], apart[:, 1, :], ALU.add))
                    st.sync()
                    dve.wait_ge(ph.q2, s * QB + QB)
                    for q in range(QB):
                        for k in range(KD):
                            last = ts((KK, Tm)[q][:, k, :], QQ[:, q, k, :], Acol[:, k:k + 1], None, ALU.mult)
                        last.then_inc(ph.mixed, 1)
                    for q in range(QB):
                        b = s * QB + q
                        dve.wait_ge(ph.mix_hi, b + 1)
                        tt(HL[:, 1, :, :], (KK, Tm)[q][:, :, :], HL[:, 0, :, :].bitcast(F32), ALU.subtract).then_inc(ph.mix_lo, 1)
                        dve.wait_ge(ph.mix_lo, b + 1)
                        dve.wait_ge(ph.y, b + 1)
                        for k in range(KD):
                            st.do(stt(KK[:, k, :], ps[:, YB + k, :], col("b_out", k), XR[:, q, k, :], ALU.add, ALU.add))
                        st.sync()
                        tt(xblock(b), xblock(b), KK[:, :, :], ALU.add).then_inc(x_ready, 1)
                        dve.wait_ge(x_ready, 5 * NB + b + 1)

            route0 = lambda n: lambda: route(F0, L0, n)
            route1 = lambda n: lambda: route(F1, L1, n)
            route0(0)()
            slot(L0, F0, 0, 0, 0, NB, route0(1))
            with dve.Fori(1, NB + 1) as n:
                t, xr = L0.C + (n - 1) * B_ITEMS, NB + 2 * n - 1
                slot(L0, F0, n, t, n, xr, None, attn0(A0, F0, n, t, n, xr, route0(n + 1)))
            with dve.Fori(NB + 1, JOBS - 1) as n:
                slot(L0, F0, n, n * L0.C + NB * A0_HID, n, 2 * NB + n, route0(n + 1))
            n = JOBS - 1
            slot(L0, F0, n, LAST0, n, 2 * NB + n, route1(0))
            with dve.Fori(0, NB - 1) as n:
                slot(L1, F1, n, n * L1.C, JOBS + n, 4 * NB + n, route1(n + 1))
            n = NB - 1
            slot(L1, F1, n, n * L1.C, JOBS + n, 4 * NB + n, None)
            attn1(A1)
            route1(NB)()
            with dve.Fori(NB, JOBS - 1) as n:
                slot(L1, F1, n, n * L1.C, JOBS + NB + n, 5 * NB + n, route1(n + 1), final=True)
            n = JOBS - 1
            slot(L1, F1, n, n * L1.C, JOBS + NB + n, 5 * NB + n, None, final=True)


def chunks(gate, up, down, per):
    import numpy as np
    E, _, H = gate.shape
    C = H // per
    def io(w):
        w = w.reshape(E, KD, P, C, per).transpose(3, 2, 1, 0, 4)
        return w.reshape(C, P, KD * P)
    d = down.reshape(E, C, per, D).transpose(1, 0, 2, 3).reshape(C, P, D)
    return np.concatenate([io(gate), io(up), d], axis=2)


def padded(w, axis, n):
    import numpy as np
    widths = [(0, 0)] * w.ndim
    widths[axis] = (0, n - w.shape[axis])
    return np.pad(w, widths)


def ffn_weights(gate, up, down, sgate, sup, sdown, f):
    import numpy as np
    n = f.shared * P
    s = chunks(padded(sgate, 1, n)[None], padded(sup, 1, n)[None], padded(sdown, 0, n)[None], P)
    return np.ascontiguousarray(np.concatenate([s, chunks(gate, up, down, f.per)], axis=0))


def by_k(w):
    return w.reshape(KD, P, -1).transpose(1, 0, 2).reshape(P, -1)


def kernel(**inputs):
    import numpy as np
    import concourse.bacc as bacc
    from concourse.bass_utils import run_bass_kernel_spmd

    a = {k: np.asarray(v) for k, v in inputs.items()}
    g = lambda n: a["L0_attn_" + n]
    w0 = ffn_weights(*[a["L0_ffn_" + n] for n in ("w_gate", "w_up", "w_down", "sw_gate", "sw_up", "sw_down")], L0)
    w1 = ffn_weights(*[a["L1_ffn_" + n] for n in ("wg", "wu", "wd", "sg", "su", "sd")], L1)
    square = [by_k(g(n).T) for n in ("Wk", "Wv", "Wr", "Wo", "Wcr")]
    hid = [np.concatenate([by_k(g("Wkey").T[:, j * P:(j + 1) * P]), g("Wval").T[j * P:(j + 1) * P]], axis=1)
           for j in range(A0_HID)]
    wa0 = np.ascontiguousarray(np.stack(square + hid))
    pair = np.arange(P) ^ 1
    rows = {"Q1": np.arange(P), "RQ": pair, "Q2": P + np.arange(P), "K1": D + np.arange(P), "RK": D + pair,
            "K2": D + P + np.arange(P), "V1": 2 * D + np.arange(P), "V2": 2 * D + P + np.arange(P)}
    sel = np.concatenate([rows[n] for n in ("K1", "RK", "K2", "V1", "V2", "Q1", "RQ", "Q2")])
    win = a["L1_attn_W_in"][sel].T
    wa1 = np.ascontiguousarray(np.stack([by_k(win[:, i * D:(i + 1) * D]) for i in range(4)] + [by_k(a["L1_attn_W_out"].T)]))
    flat = lambda v: v.reshape(-1, P).T
    names = {n: g(n) for n in ("ln1_g", "ln1_b", "ln2_g", "ln2_b", "tm_first", "tm_mk", "tm_mv", "tm_mr", "cm_mk", "cm_mr")}
    names["b_out"] = a["L1_attn_b_out"]
    vecs = np.ascontiguousarray(np.concatenate([flat(names[n]) for n in VEC] + [flat(a["L1_attn_b_in"][sel])], axis=1))
    half = D // 2
    inv = (np.float32(1.0) / np.float32(10000.0) ** (np.arange(0, half, 2, dtype=np.float32) / np.float32(half))).astype(np.float32)
    freq = np.repeat(np.arange(SEQ, dtype=np.float32)[:, None] * inv[None, :], 2, axis=1).T
    sign = np.where(np.arange(P) % 2 == 0, -1.0, 1.0).astype(np.float32)[:, None]
    tables = np.stack([np.cos(freq), np.sin(freq) * sign], axis=1).astype(np.float32)
    cs = np.ascontiguousarray(tables.reshape(P, 2, QB, BT).transpose(2, 0, 1, 3))
    gate = lambda w: np.ascontiguousarray(w.reshape(KD, P, -1).transpose(1, 0, 2))
    arrays = {
        "x_in": np.ascontiguousarray(a["L0_attn_x"].reshape(NTOK, D)), "w0": w0, "w1": w1, "wa0": wa0, "wa1": wa1,
        "gate0": gate(a["L0_ffn_gate_w"]), "gate1": gate(a["L1_ffn_gate_w"]), "vecs": vecs, "cs": cs,
        "ident_in": np.eye(P, dtype=np.float32),
    }
    nc = bacc.Bacc("TRN2", target_bir_lowering=False, num_devices=1, dynamic_dma_scratch_size=512)
    aps = {n: nc.dram_tensor(n, v.shape, F32, kind="ExternalInput").ap() for n, v in arrays.items()}
    out = nc.dram_tensor("out", (NTOK, D), F32, kind="ExternalOutput").ap()
    program(nc, out=out, **aps)
    r = run_bass_kernel_spmd(nc, [arrays], core_ids=[0])
    return r.results[0]["out"].reshape(BATCH, SEQ, D)
```
